# Optimizing a Trainium2 kernel written in Bass

```python
import numpy as np
import jax
import jax.numpy as jnp

def _softmax(x, axis=-1):
    return jax.nn.softmax(x, axis=axis)

def _gelu(x):
    return jax.nn.gelu(x, approximate=True)

def _silu(x):
    return jax.nn.silu(x)

def _sigmoid(x):
    return jax.nn.sigmoid(x)

def _layernorm(x, axis=-1, eps=1e-05):
    m = jnp.mean(x, axis=axis, keepdims=True)
    v = jnp.var(x, axis=axis, keepdims=True)
    return (x - m) / jnp.sqrt(v + eps)

def _scatter_add(tgt, idx, src, axis=0):
    return tgt.at[idx].add(src)

def _segment_sum(src, seg, n):
    return jax.ops.segment_sum(src, seg, n)
kernel_name = 'mk_flamingo_gated_d1_seqx_r8_3669c9'

def setup_inputs(seed: int=0):
    np.random.seed(seed)
    _w = jnp.asarray

    def _rec_inputs():
        import jax
        import jax.numpy as jnp
        _rk = jax.random.key(seed)
        x = 7.22e-05 + 1 * jax.random.normal(jax.random.fold_in(_rk, 1), (32, 128, 128), jnp.float32)
        _lenS = 128 - jax.random.randint(jax.random.fold_in(_rk, 7), (32,), 0, max(1, 128 // 4) + 1, jnp.int32)
        _lenS2 = 120 - jax.random.randint(jax.random.fold_in(_rk, 8), (32,), 0, max(1, 120 // 4) + 1, jnp.int32)
        _ctx_1024P = jax.random.normal(jax.random.fold_in(_rk, 11), (32, 16, 128), jnp.float32)
        _ctx_1024c = jax.random.dirichlet(jax.random.fold_in(_rk, 511), 0.3 * jnp.ones((16,), jnp.float32), (32, 120))
        _ctx_1024t = jnp.einsum('bsk,bkd->bsd', _ctx_1024c, _ctx_1024P)
        _ctx_1024t = _ctx_1024t * jax.lax.rsqrt(jnp.mean(jnp.square(_ctx_1024t)) + 1e-12) * 0.953939
        ctx_1024 = 4.13588e-05 + 0.999923 * (_ctx_1024t + 0.3 * jax.random.normal(jax.random.fold_in(_rk, 611), (32, 120, 128), jnp.float32))
        _validS = jnp.arange(128)[None, :] < _lenS[:, None]
        _validS2 = jnp.arange(120)[None, :] < _lenS2[:, None]
        _causal = jnp.tril(jnp.ones((128, 128), dtype=bool))
        mask_SxS2_ik0 = jnp.where(jnp.broadcast_to(_validS2[0:1, :], (128, 120)), 0, 1).astype(jnp.int32)
        _g = jax.random.normal(jax.random.fold_in(_rk, 9001), (2, 1), jnp.float32)
        _g = jnp.sign(_g) * jnp.maximum(jnp.abs(_g), 1.0) + (_g == 0) * 1.0
        g_xattn = _g[0]
        g_ffn = _g[1]
        return (x, ctx_1024, mask_SxS2_ik0, g_xattn, g_ffn)
    x, ctx_1024, mask_SxS2_ik0, g_xattn, g_ffn = _rec_inputs()

    def _L0_xattn_setup():
        import jax, jax.numpy as jnp
        import numpy as np
        D_MODEL = 128
        N_HEADS = 16
        D_K = D_MODEL // N_HEADS
        B, L = (4, 256)
        key = jax.random.key(seed)
        ks = jax.random.split(key, 12)
        s_in = 1.0 / np.sqrt(D_MODEL)
        inp = {'Q': jax.random.normal(ks[0], (B, L, D_MODEL), jnp.float32), 'K': jax.random.normal(ks[1], (B, L, D_MODEL), jnp.float32), 'V': jax.random.normal(ks[2], (B, L, D_MODEL), jnp.float32), 'attn_mask': jnp.tril(jnp.ones((L, L), jnp.int32)), 'Wq': jax.random.normal(ks[3], (D_MODEL, D_MODEL), jnp.float32) * s_in, 'bq': jnp.zeros((D_MODEL,), jnp.float32), 'Wk': jax.random.normal(ks[4], (D_MODEL, D_MODEL), jnp.float32) * s_in, 'bk': jnp.zeros((D_MODEL,), jnp.float32), 'Wv': jax.random.normal(ks[5], (D_MODEL, D_MODEL), jnp.float32) * s_in, 'bv': jnp.zeros((D_MODEL,), jnp.float32), 'Wo': jax.random.normal(ks[6], (D_MODEL, D_MODEL), jnp.float32) * s_in, 'bo': jnp.zeros((D_MODEL,), jnp.float32)}
        return inp
    _L0_xattn_all = _L0_xattn_setup()
    _L0_xattn_in = {k: v for k, v in _L0_xattn_all.items() if k in ('Wq', 'bq', 'Wk', 'bk', 'Wv', 'bv', 'Wo', 'bo')}
    del _L0_xattn_all

    def _L0_ffn_setup():
        import jax, jax.numpy as jnp
        import numpy as np
        D_MODEL = 128
        D_FF = 512
        N_EXPERTS = 8
        TOP_K = 2
        S, B = (256, 4)
        key = jax.random.key(seed)
        ks = jax.random.split(key, 7)
        sc_in = 1.0 / np.sqrt(D_MODEL)
        sc_ff = 1.0 / np.sqrt(D_FF)
        return {'x': jax.random.normal(ks[0], (S, B, D_MODEL), dtype=jnp.float32), 'gate_w': jax.random.uniform(ks[1], (D_MODEL, N_EXPERTS), jnp.float32, -sc_in, sc_in), 'gate_b': jnp.zeros((N_EXPERTS,), jnp.float32), 'w1': jax.random.uniform(ks[2], (N_EXPERTS, D_MODEL, D_FF), jnp.float32, -sc_in, sc_in), 'b1': jax.random.uniform(ks[3], (N_EXPERTS, D_FF), jnp.float32, -sc_in, sc_in), 'w2': jax.random.uniform(ks[4], (N_EXPERTS, D_FF, D_MODEL), jnp.float32, -sc_ff, sc_ff), 'b2': jax.random.uniform(ks[5], (N_EXPERTS, D_MODEL), jnp.float32, -sc_ff, sc_ff)}
    _L0_ffn_all = _L0_ffn_setup()
    _L0_ffn_in = {k: v for k, v in _L0_ffn_all.items() if k in ('gate_w', 'gate_b', 'w1', 'b1', 'w2', 'b2')}
    del _L0_ffn_all
    return {'x': x, 'ctx_1024': ctx_1024, 'mask_SxS2_ik0': mask_SxS2_ik0, 'g_xattn': g_xattn, 'g_ffn': g_ffn, 'L0_xattn_Wq': _L0_xattn_in['Wq'], 'L0_xattn_bq': _L0_xattn_in['bq'], 'L0_xattn_Wk': _L0_xattn_in['Wk'], 'L0_xattn_bk': _L0_xattn_in['bk'], 'L0_xattn_Wv': _L0_xattn_in['Wv'], 'L0_xattn_bv': _L0_xattn_in['bv'], 'L0_xattn_Wo': _L0_xattn_in['Wo'], 'L0_xattn_bo': _L0_xattn_in['bo'], 'L0_ffn_gate_w': _L0_ffn_in['gate_w'], 'L0_ffn_gate_b': _L0_ffn_in['gate_b'], 'L0_ffn_w1': _L0_ffn_in['w1'], 'L0_ffn_b1': _L0_ffn_in['b1'], 'L0_ffn_w2': _L0_ffn_in['w2'], 'L0_ffn_b2': _L0_ffn_in['b2']}

def reference(x, ctx_1024, mask_SxS2_ik0, g_xattn, g_ffn, L0_xattn_Wq, L0_xattn_bq, L0_xattn_Wk, L0_xattn_bk, L0_xattn_Wv, L0_xattn_bv, L0_xattn_Wo, L0_xattn_bo, L0_ffn_gate_w, L0_ffn_gate_b, L0_ffn_w1, L0_ffn_b1, L0_ffn_w2, L0_ffn_b2):
    import jax
    import jax.numpy as jnp

    def _L0_xattn_ref(Q, K, V, Wq, bq, Wk, bk, Wv, bv, Wo, bo, attn_mask):
        import jax, jax.numpy as jnp
        import numpy as np
        D_MODEL = 128
        N_HEADS = 16
        D_K = D_MODEL // N_HEADS
        B, L = (4, 256)
        Bq, Lq, D = Q.shape
        Lk = K.shape[1]
        q = (Q @ Wq.T + bq).reshape(Bq, Lq, N_HEADS, D_K).transpose(0, 2, 1, 3)
        k = (K @ Wk.T + bk).reshape(Bq, Lk, N_HEADS, D_K).transpose(0, 2, 1, 3)
        v = (V @ Wv.T + bv).reshape(Bq, Lk, N_HEADS, D_K).transpose(0, 2, 1, 3)
        scores = jnp.einsum('bhqd,bhkd->bhqk', q, k) / jnp.sqrt(jnp.float32(D_K))
        mask = attn_mask[None, None, :, :]
        scores = jnp.where(mask == 0, jnp.float32(-jnp.inf), scores)
        attn = jax.nn.softmax(scores, axis=-1)
        out = jnp.einsum('bhqk,bhkd->bhqd', attn, v)
        out = out.transpose(0, 2, 1, 3).reshape(Bq, Lq, D)
        return out @ Wo.T + bo

    def _L0_ffn_ref(x, gate_w, gate_b, w1, b1, w2, b2):
        import jax, jax.numpy as jnp
        import numpy as np
        D_MODEL = 128
        D_FF = 512
        N_EXPERTS = 8
        TOP_K = 2
        S, B = (256, 4)
        s, b, d = x.shape
        T = s * b
        x_flat = x.reshape(T, d)
        scores = x_flat @ gate_w + gate_b
        topk_vals, topk_idx = jax.lax.top_k(scores, TOP_K)
        topk_probs = jax.nn.softmax(topk_vals, axis=-1)
        tok = jnp.arange(T)[:, None]
        combine_w = jnp.zeros((T, N_EXPERTS), x.dtype).at[tok, topk_idx].add(topk_probs)
        h = jax.nn.relu(jnp.einsum('td,edf->etf', x_flat, w1) + b1[:, None, :])
        y = jnp.einsum('etf,efd->etd', h, w2) + b2[:, None, :]
        out = jnp.einsum('te,etd->td', combine_w, y)
        return out.reshape(s, b, d)
    x = x + jnp.tanh(g_xattn[0]) * _L0_xattn_ref(_layernorm(x, axis=-1), ctx_1024, ctx_1024, L0_xattn_Wq, L0_xattn_bq, L0_xattn_Wk, L0_xattn_bk, L0_xattn_Wv, L0_xattn_bv, L0_xattn_Wo, L0_xattn_bo, mask_SxS2_ik0)
    x = x + jnp.tanh(g_ffn[0]) * _L0_ffn_ref(_layernorm(x, axis=-1), L0_ffn_gate_w, L0_ffn_gate_b, L0_ffn_w1, L0_ffn_b1, L0_ffn_w2, L0_ffn_b2)
    return x

_drawn_inputs = setup_inputs


def setup_inputs(seed=0):
    import zlib

    import numpy as np

    out = dict(_drawn_inputs(seed))
    spreads = {'L0_xattn_bq': (0.0, 0.279),
     'L0_xattn_bk': (0.0, 0.8),
     'L0_xattn_bv': (0.0, 0.1),
     'L0_xattn_bo': (0.0, 0.1),
     'L0_ffn_gate_b': (0.0, 0.1)}
    factors = {'L0_ffn_b1': 4.807, 'L0_ffn_b2': 3.967}
    for name, (base, spread) in spreads.items():
        noise = np.random.default_rng([zlib.crc32(name.encode()), seed]).standard_normal(out[name].shape)
        drawn = base * np.exp(spread * noise) if base else spread * noise
        out[name] = jnp.asarray(drawn.astype(out[name].dtype))
    for name, factor in factors.items():
        out[name] = (out[name] * factor).astype(out[name].dtype)
    return out
```

```python
from contextlib import ExitStack

import concourse.bass as bass
from concourse import mybir

F32 = mybir.dt.float32
F32R = mybir.dt.float32r
I32 = mybir.dt.int32
U32 = mybir.dt.uint32
ALU = mybir.AluOpType
ACT = mybir.ActivationFunctionType
AX_X = mybir.AxisListType.X

B, LQ, D = 32, 128, 128
LK = 120
NH, DK = 16, 8
NE, FF = 8, 512
NC = FF // 128
GB = 4
NG = B // GB
HG = 4
NHG = NH // HG
NP = GB * NHG
TOK = GB * LQ
KEYS = GB * LK
EPS = 1e-5
MASKED = -1e30

U_Z, U_CTX, U_K, U_Q, U_V, U_S = 0, 1, 2, 6, 10, 12
AUSE = U_S + NP
NHI = U_V
NCH = NE * NC
LAG = 3
FMUSE = 3 + NE + 1
ROUTE = 16
TLAG = 3
VLAG = TLAG + 1
SLOTS = NP + VLAG + 1
NEXT_USES = {NP + _k: [2 * _k, 2 * _k + 1] for _k in range(5)}
KEYS0_SLOT = NP + 3
STEP_COUNTS = [1, 2, 2, 2, 1, 2, 2, 2, 1, 2, 2, 2, 1, 2, 2, 2, 2, 1, 2, 2]
STEP_SLOTS = len(STEP_COUNTS)
assert sum(STEP_COUNTS) == NCH + LAG and STEP_SLOTS <= SLOTS
SLOT_STEPS = [list(range(sum(STEP_COUNTS[:_s]), sum(STEP_COUNTS[:_s + 1]))) for _s in range(SLOTS)]
ROUTE_1, ROUTE_2, COMB_SLOT = 0, 1, 3
BEHIND = 1
RESULT_SLOT = SLOTS - 1


def steps_behind(s):
    return [n - BEHIND for n in SLOT_STEPS[s] if n >= BEHIND]


def experts_done_at(n):
    e, r = divmod(n - LAG - NC, NC)
    return e if r == 0 and e >= 0 else None


def closes_batch(s):
    i, r = divmod(s - VLAG - NHG, NHG)
    return i if r == 0 and 0 <= i < GB else None


def at(group, per_group, k):
    return group * per_group + k


def wait(eng, sem, value):
    if not isinstance(value, int) or value > 0:
        eng.wait_ge(sem, value)


def build(nc, x, ctx, mask, g_x, g_f, wq, bq, wk, bk, wv, bv, wo, bo, gate_w, gate_b, w1, b1, w2, b2,
          ident, sel, iota, hmask, out):
    with ExitStack() as es:
        def sb(name, shape, dt=F32):
            return es.enter_context(nc.sbuf_tensor(name, shape, dt))

        def ps(name):
            return es.enter_context(nc.psum_tensor(name, [128, 512], F32))

        def sem(name):
            return es.enter_context(nc.semaphore(name))

        X = sb("X", [128, B, D])
        I = sb("I", [128, 128])
        iota_sb = sb("iota_sb", [128, NE])
        hm = sb("hm", [128, HG])
        sel_r = sb("sel_r", [2 * NE, NE, 128], F32R)
        mbias = sb("mbias", [128, LK])
        mtmp = sb("mtmp", [128, 4])
        gx = sb("gx", [128, 1])
        gf = sb("gf", [128, 1])
        tx = sb("tx", [128, 1])
        tf = sb("tf", [128, 1])
        wq_h = sb("wq_h", [128, NHG, 128], F32R)
        wq_l = sb("wq_l", [128, NHG, 128], F32R)
        wk_h = sb("wk_h", [128, NHG, 128], F32R)
        wk_l = sb("wk_l", [128, NHG, 128], F32R)
        bq_sb = sb("bq_sb", [128, NHG])
        bk_sb = sb("bk_sb", [128, NHG])
        wv_h = sb("wv_h", [128, D], F32R)
        wv_l = sb("wv_l", [128, D], F32R)
        bv_sb = sb("bv_sb", [128, 1])
        wo_sb = sb("wo_sb", [128, D])
        bo_sb = sb("bo_sb", [128, D])
        wg_raw = sb("wg_raw", [128, NE])
        wg_h = sb("wg_h", [128, NE], F32R)
        wg_l = sb("wg_l", [128, NE], F32R)
        bg_sb = sb("bg_sb", [128, NE])
        w_raw = sb("w_raw", [128, 2, FF])
        w1_h = sb("w1_h", [128, NE, FF], F32R)
        w1_l = sb("w1_l", [128, NE, FF], F32R)
        w2_h = sb("w2_h", [128, NE, NC * D], F32R)
        w2_l = sb("w2_l", [128, NE, NC * D], F32R)
        b1_sb = sb("b1_sb", [128, NE * NC])
        b2_sb = sb("b2_sb", [128, NE])
        eps4 = sb("eps4", [128, GB])
        mhalf4 = sb("mhalf4", [128, GB])
        ctx_sb = sb("ctx_sb", [LK, GB, D])
        stat1 = sb("stat1", [128, GB, 6])
        mv1 = sb("mv1", [128, GB, 2])
        rstd1 = sb("rstd1", [128, 2, GB])
        stat2 = sb("stat2", [128, GB, 6])
        mv2 = sb("mv2", [128, GB, 2])
        rstd2 = sb("rstd2", [128, 2, GB])
        z1 = sb("z1", [128, GB, D])
        z2 = sb("z2", [128, GB, D])
        zT_h = sb("zT_h", [128, TOK], F32R)
        zT_l = sb("zT_l", [128, TOK], F32R)
        cT_h = sb("cT_h", [128, KEYS], F32R)
        cT_l = sb("cT_l", [128, KEYS], F32R)
        Qs = sb("Qs", [128, NHG, TOK], F32R)
        Ks = sb("Ks", [128, NHG, KEYS], F32R)
        Kb = sb("Kb", [128, 2, NHG, HG, LK], F32R)
        Vm = sb("Vm", [LK, GB, NH * 32])
        SM = sb("SM", [128, 2, HG, LK])
        nmax = sb("nmax", [128, 4, HG])
        P = sb("P", [128, 4, HG, LK])
        sums = sb("sums", [128, 4, HG])
        rec = sb("rec", [128, 4, HG])
        PT = sb("PT", [LK, 2, HG * LQ])
        OT = sb("OT", [128, LQ])
        xb = sb("xb", [128, GB, D])
        z2T_h = sb("z2T_h", [128, TOK], F32R)
        z2T_l = sb("z2T_l", [128, TOK], F32R)
        gs = sb("gs", [128, GB, NE])
        top = sb("top", [128, GB, 8])
        idx = sb("idx", [128, GB, 8], U32)
        idxf = sb("idxf", [128, GB, 2])
        diff = sb("diff", [128, GB])
        ediff = sb("ediff", [128, GB])
        esum = sb("esum", [128, GB])
        p1 = sb("p1", [128, 2, GB])
        p2 = sb("p2", [128, GB])
        eq1 = sb("eq1", [128, 2, GB, NE])
        eq2 = sb("eq2", [128, 2, GB, NE])
        comb = sb("comb", [128, GB, NE])
        c2 = sb("c2", [128, GB, 2 * NE])
        cmbT = sb("cmbT", [2 * NE, TOK], F32R)
        H = sb("H", [128, 4, TOK])
        H_h = sb("H_h", [128, 4, TOK], F32R)
        H_l = sb("H_l", [128, 4, TOK], F32R)
        yb = sb("yb", [128, TOK])
        wy = sb("wy", [128, TOK])
        acc = sb("acc", [128, TOK])

        spare = sb("spare", [128, 1])
        wk_raw = yb[:].rearrange("p (g r) -> p g r", g=NHG)
        wq_raw = wy[:].rearrange("p (g r) -> p g r", g=NHG)
        wv_raw = z2[:, 0, :]
        mask_i = P[:, 0, 0, :].bitcast(I32)
        sel_raw = H[0:2 * NE, 0:2, :].rearrange("s a (e p) -> s (a e) p", p=128)

        A = [ps("A0"), ps("A1")]
        Tb = ps("T")
        Ob = ps("O")
        Ub = [ps("U0"), ps("U1")]
        Yb = ps("Y")
        Fb = ps("F")

        in_first = sem("in_first")
        in_const = sem("in_const")
        in_x = sem("in_x")
        in_ctx = sem("in_ctx")
        in_w = [sem(f"in_w{r}") for r in range(2)]
        out_done = sem("out_done")
        prep_dve = sem("prep_dve")
        tanh_done = sem("tanh_done")
        const_done = sem("const_done")
        whi_done = sem("whi_done")
        wlo_done = sem("wlo_done")
        a_ready = sem("a_ready")
        a_free = sem("a_free")
        hi_done = sem("hi_done")
        ln1_step = sem("ln1_step")
        rstd1_done = sem("rstd1_done")
        z1_done = sem("z1_done")
        kb_done = sem("kb_done")
        max_done = sem("max_done")
        exp_done = sem("exp_done")
        rec_done = sem("rec_done")
        norm_done = sem("norm_done")
        t_ready = sem("t_ready")
        pt_done = sem("pt_done")
        pv_done = sem("pv_done")
        ot_done = sem("ot_done")
        proj_done = sem("proj_done")
        xb_done = sem("xb_done")
        x1_done = sem("x1_done")
        ln2_step = sem("ln2_step")
        rstd2_done = sem("rstd2_done")
        z2_done = sem("z2_done")
        f_ready = sem("f_ready")
        z2hi_done = sem("z2hi_done")
        z2lo_done = sem("z2lo_done")
        route_step = sem("route_step")
        ediff_done = sem("ediff_done")
        cmbT_done = sem("cmbT_done")
        u_ready = sem("u_ready")
        h_done = sem("h_done")
        hhi_done = sem("hhi_done")
        hlo_done = sem("hlo_done")
        y_ready = sem("y_ready")
        yb_done = sem("yb_done")
        wy_done = sem("wy_done")
        acc_done = sem("acc_done")
        fin_done = sem("fin_done")

        block = es.enter_context(nc.Block())

        N_FIRST = 16 * 8
        N_CONST = 16 * 14
        N_XREST = 16

        def group_x(G):
            if isinstance(G, int):
                return X[:, G * GB:(G + 1) * GB, :]
            return X[:, bass.ds(G * GB, GB), :]

        def batch_x(G, i):
            if isinstance(G, int):
                return X[:, G * GB + i, :]
            return X[:, bass.ds(G * GB + i, 1), :].squeeze(1)

        @block.sync
        def _(sp):
            sp.dma_start(X[:, 0:GB, :], x[0:GB].rearrange("b q d -> q b d")).then_inc(in_first, 16)
            sp.dma_start(ctx_sb[:], ctx[0:GB].rearrange("b k d -> k b d")).then_inc(in_ctx, 16)
            for dst, src in ((I[:], ident), (wk_raw, wk), (bk_sb[:], bk), (wq_raw, wq), (bq_sb[:], bq), (hm[:], hmask),
                             (wv_raw, wv)):
                sp.dma_start(dst, src).then_inc(in_first, 16)
            sp.dma_start(mask_i, mask).then_inc(in_const, 16)
            for dst, src in ((gx, g_x), (gf, g_f), (bo_sb, bo), (bg_sb, gate_b), (iota_sb, iota)):
                sp.dma_start(dst[:], src.partition_broadcast(128)).then_inc(in_const, 16)
            for dst, src in ((wo_sb[:], wo), (bv_sb[:], bv), (wg_raw[:], gate_w), (sel_raw, sel), (b1_sb[:], b1),
                             (b2_sb[:], b2)):
                sp.dma_start(dst, src).then_inc(in_const, 16)
            sp.dma_start(X[:, GB:B, :], x[GB:B].rearrange("b q d -> q b d")).then_inc(in_x, 16)

            for k in range(2 * NE):
                if k >= 2:
                    sp.wait_ge(wlo_done, k - 1)
                src = w1[k] if k < NE else w2[k - NE].rearrange("(c p) d -> p c d", p=128)
                dst = w_raw[:, k % 2, :] if k < NE else w_raw[:, k % 2, :].rearrange("p (c d) -> p c d", c=NC)
                sp.dma_start(dst, src).then_inc(in_w[k % 2], 16)
                if k == 1:
                    sp.wait_ge(a_ready, U_CTX + 1)
                    sp.dma_start(ctx_sb[:], ctx[GB:2 * GB].rearrange("b k d -> k b d")).then_inc(in_ctx, 16)

            def body(G, more):
                if more:
                    sp.wait_ge(a_ready, at(G, AUSE, U_CTX + 1))
                    src = ctx[(G + 1) * GB:(G + 2) * GB] if isinstance(G, int) else ctx[bass.ds((G + 1) * GB, GB)]
                    sp.dma_start(ctx_sb[:], src.rearrange("b k d -> k b d")).then_inc(in_ctx, 16)
                sp.wait_ge(fin_done, G)
                dst = out[(G - 1) * GB:G * GB] if isinstance(G, int) else out[bass.ds((G - 1) * GB, GB)]
                sp.dma_start(dst.rearrange("b q d -> q b d"), group_x(G - 1)).then_inc(out_done, 16)

            with sp.Fori(1, NG - 1) as G:
                body(G, True)
            body(NG - 1, False)
            body(NG, False)
            sp.wait_ge(out_done, 16 * NG)

        @block.tensor
        def _(pe):
            mm = nc.tensor.matmul

            def split_product(dst, w_h, w_l, v_h, v_l, **kw):
                mm(dst, w_h, v_h, start=True, stop=False)
                mm(dst, w_l, v_h, start=False, stop=False)
                return mm(dst, w_h, v_l, start=False, stop=True)

            def prep_use(G, u):
                wait(pe, a_free, at(G, AUSE, u - 1))
                bank = A[u % 2]
                if u == U_Z:
                    pe.wait_ge(z1_done, at(G, 1, 1))
                    for i in range(GB):
                        last = nc.tensor.transpose(bank[:, i * LQ:(i + 1) * LQ], z1[:, i, :], I[:])
                elif u == U_CTX:
                    pe.wait_ge(in_ctx, at(G, 16, 16))
                    for i in range(GB):
                        last = nc.tensor.transpose(bank[:, i * LK:(i + 1) * LK], ctx_sb[:, i, :], I[0:LK, 0:LK])
                elif u < U_Q:
                    g = u - U_K
                    pe.wait_ge(a_free, at(G, AUSE, U_CTX + 1))
                    last = split_product(bank[:, 0:KEYS], wk_h[:, g, :], wk_l[:, g, :], cT_h[:], cT_l[:])
                elif u < U_V:
                    g = u - U_Q
                    last = split_product(bank[:], wq_h[:, g, :], wq_l[:, g, :], zT_h[:], zT_l[:])
                else:
                    for i in range(2):
                        k0 = ((u - U_V) * 2 + i) * LK
                        last = split_product(bank[0:LK, i * D:(i + 1) * D], cT_h[:, k0:k0 + LK],
                                             cT_l[:, k0:k0 + LK], wv_h[:], wv_l[:])
                last.then_inc(a_ready, 1)

            def scores(G, p):
                i, g = divmod(p, NHG)
                u = U_S + p
                pe.wait_ge(a_free, at(G, AUSE, u - 1))
                if g == 0:
                    pe.wait_ge(kb_done, at(G, GB, i + 1))
                mm(A[u % 2][:, 0:HG * LK], Qs[:, g, i * LQ:(i + 1) * LQ],
                   Kb[:, i % 2, g, :, :].rearrange("p j k -> p (j k)"), start=True, stop=True).then_inc(a_ready, 1)

            def transposes(G, p):
                pe.wait_ge(norm_done, at(G, NP, p + 1))
                wait(pe, pt_done, at(G, NP, p))
                for j in range(HG):
                    last = nc.tensor.transpose(Tb[0:LK, j * LQ:(j + 1) * LQ], P[:, p % 4, j, :], I[:])
                last.then_inc(t_ready, 1)

            def values(G, p):
                i, g = divmod(p, NHG)
                pe.wait_ge(pt_done, at(G, NP, p + 1))
                if g == 0:
                    wait(pe, x1_done, at(G, GB, i))
                for j in range(HG):
                    c0 = (j * NHG + g) * 32
                    last = mm(Ob[32 * j:32 * j + 32, 0:LQ], Vm[:, i, c0:c0 + 32], PT[:, p % 2, j * LQ:(j + 1) * LQ],
                              start=(g == 0), stop=(g == NHG - 1), tile_position=(0, 32 * j))
                last.then_inc(pv_done, 1)

            def project(G, i):
                pe.wait_ge(ot_done, at(G, GB, i + 1))
                mm(Ob[:, LQ:LQ + D], OT[:], wo_sb[:], start=True, stop=True).then_inc(proj_done, 1)

            def z2_transposes(F):
                pe.wait_ge(z2_done, at(F, 1, 1))
                for i in range(GB):
                    last = nc.tensor.transpose(Fb[:, i * LQ:(i + 1) * LQ], z2[:, i, :], I[:])
                last.then_inc(f_ready, 1)

            def gate(F):
                pe.wait_ge(z2lo_done, at(F, 1, 1))
                for i in range(GB):
                    t = slice(i * LQ, (i + 1) * LQ)
                    last = split_product(Fb[:, i * NE:(i + 1) * NE], z2T_h[:, t], z2T_l[:, t], wg_h[:], wg_l[:])
                last.then_inc(f_ready, 1)

            def comb_transposes(F):
                pe.wait_ge(route_step, at(F, ROUTE, ROUTE))
                for i in range(GB):
                    last = nc.tensor.transpose(Fb[0:2 * NE, i * LQ:(i + 1) * LQ], c2[:, i, :], I[:])
                last.then_inc(f_ready, 1)

            def spread(F, e):
                if e == 0:
                    pe.wait_ge(cmbT_done, at(F, 1, 1))
                else:
                    pe.wait_ge(wy_done, at(F, NE, e))
                mm(Fb[:], sel_r[:, e, :], cmbT[:], start=True, stop=True).then_inc(f_ready, 1)

            def step(F, n):
                if n < NCH:
                    e, c = divmod(n, NC)
                    if n >= 2:
                        wait(pe, h_done, at(F, NCH, n - 1))
                    split_product(Ub[n % 2][:], w1_h[:, e, c * 128:(c + 1) * 128], w1_l[:, e, c * 128:(c + 1) * 128],
                                  z2T_h[:], z2T_l[:]).then_inc(u_ready, 1)
                if n >= LAG:
                    m = n - LAG
                    e, c = divmod(m, NC)
                    if c == 0 and e > 0:
                        wait(pe, yb_done, at(F, NE, e))
                    pe.wait_ge(hlo_done, at(F, NCH, m + 1))
                    d = slice(c * D, (c + 1) * D)
                    mm(Yb[:], w2_h[:, e, d], H_h[:, m % 4, :], start=(c == 0), stop=False)
                    mm(Yb[:], w2_l[:, e, d], H_h[:, m % 4, :], start=False, stop=False)
                    last = mm(Yb[:], w2_h[:, e, d], H_l[:, m % 4, :], start=False, stop=(c == NC - 1))
                    if c == NC - 1:
                        last.then_inc(y_ready, 1)
                if n >= LAG + NC - 1 and (n - LAG - NC + 1) % NC == 0:
                    spread(F, (n - LAG - NC + 1) // NC)

            def result_transposes(F):
                pe.wait_ge(acc_done, at(F, NE - 1, NE - 1))
                for i in range(GB):
                    last = nc.tensor.transpose(Fb[:, i * LQ:(i + 1) * LQ], acc[:, i * LQ:(i + 1) * LQ], I[:])
                last.then_inc(f_ready, 1)

            def body(G, att, ffn, nxt):
                F = G - 1
                if att:
                    prep_use(G, U_V)
                    prep_use(G, U_V + 1)
                if ffn:
                    z2_transposes(F)
                for s in range(SLOTS):
                    ns = SLOT_STEPS[s] if ffn else []
                    if att and s == 0:
                        scores(G, 0)
                    if ffn and s == 0:
                        gate(F)
                    if ffn and s == COMB_SLOT:
                        comb_transposes(F)
                    us = NEXT_USES.get(s, []) if nxt else []
                    for u in us[:1]:
                        prep_use(G + 1, u)
                    if att and closes_batch(s) is not None:
                        project(G, closes_batch(s))
                    for u in us[1:]:
                        prep_use(G + 1, u)
                    for n in ns[:1]:
                        step(F, n)
                    if att and s + 1 < NP:
                        scores(G, s + 1)
                    if att and 0 <= s - TLAG < NP:
                        transposes(G, s - TLAG)
                    if att and 0 <= s - VLAG < NP:
                        values(G, s - VLAG)
                    for n in ns[1:]:
                        step(F, n)
                    if ffn and s == RESULT_SLOT:
                        result_transposes(F)

            pe.wait_ge(in_first, N_FIRST)
            pe.wait_ge(prep_dve, 12)
            for u in range(U_V):
                prep_use(0, u)
            body(0, True, False, True)
            pe.wait_ge(wlo_done, 2 * NE)
            with pe.Fori(1, NG - 1) as G:
                body(G, True, True, True)
            body(NG - 1, True, True, False)
            body(NG, False, True, False)

        @block.scalar
        def _(act):
            def prep_use(G, u):
                act.wait_ge(a_ready, at(G, AUSE, u + 1))
                bank = A[u % 2]
                if u == U_Z:
                    ins = nc.scalar.copy(zT_h[:], bank[:])
                elif u == U_CTX:
                    ins = nc.scalar.copy(cT_h[:], bank[:, 0:KEYS])
                elif u < U_Q:
                    g = u - U_K
                    ins = nc.scalar.activation(Ks[:, g, :], bank[:, 0:KEYS], ACT.Identity, bias=bk_sb[:, g:g + 1])
                else:
                    g = u - U_Q
                    ins = nc.scalar.activation(Qs[:, g, :], bank[:], ACT.Identity, bias=bq_sb[:, g:g + 1])
                ins.then_inc(hi_done, 1)

            def exps(G, p):
                act.wait_ge(max_done, at(G, NP, p + 1))
                wait(act, t_ready, at(G, NP, p - 3))
                for j in range(HG):
                    ins = nc.scalar.activation(P[:, p % 4, j, :], SM[:, p % 2, j, :], ACT.Exp,
                                               bias=nmax[:, p % 4, j:j + 1], accum_out=sums[:, p % 4, j:j + 1])
                ins.then_inc(exp_done, 1)

            def copy_pt(G, p):
                act.wait_ge(t_ready, at(G, NP, p + 1))
                wait(act, pv_done, at(G, NP, p - 1))
                nc.scalar.copy(PT[:, p % 2, :], Tb[0:LK, :]).then_inc(pt_done, 1)

            def copy_ot(G, i):
                act.wait_ge(pv_done, at(G, NP, NHG * (i + 1)))
                nc.scalar.activation(OT[:], Ob[:, 0:LQ], ACT.Identity, bias=bv_sb[:, 0:1]).then_inc(ot_done, 1)

            def hidden(F, n):
                if n < NCH:
                    act.wait_ge(u_ready, at(F, NCH, n + 1))
                    if n >= 4:
                        wait(act, hlo_done, at(F, NCH, n - 3))
                    nc.scalar.activation(H[:, n % 4, :], Ub[n % 2][:], ACT.Relu,
                                         bias=b1_sb[:, n:n + 1]).then_inc(h_done, 1)

            def step(F, n):
                hidden(F, n)
                e = experts_done_at(n + 1)
                if e is not None:
                    act.wait_ge(y_ready, at(F, NE, e + 1))
                    if e > 0:
                        act.wait_ge(wy_done, at(F, NE, e))
                    nc.scalar.activation(yb[:], Yb[:], ACT.Identity, bias=b2_sb[:, e:e + 1]).then_inc(yb_done, 1)

            def body(G, att, ffn, nxt):
                F = G - 1
                if ffn:
                    act.wait_ge(f_ready, at(F, FMUSE, 1))
                    nc.scalar.copy(z2T_h[:], Fb[:]).then_inc(z2hi_done, 1)
                for s in range(SLOTS):
                    ns = SLOT_STEPS[s] if ffn else []
                    if ffn and s == ROUTE_2:
                        act.wait_ge(route_step, at(F, ROUTE, 5))
                        nc.scalar.activation(ediff[:], diff[:], ACT.Exp).then_inc(ediff_done, 1)
                    if att and closes_batch(s) is not None:
                        copy_ot(G, closes_batch(s))
                    if nxt:
                        for u in NEXT_USES.get(s, []):
                            prep_use(G + 1, u)
                    for n in ns[:1]:
                        step(F, n)
                    if ffn and s == COMB_SLOT:
                        act.wait_ge(f_ready, at(F, FMUSE, 3))
                        nc.scalar.copy(cmbT[:], Fb[0:2 * NE, :]).then_inc(cmbT_done, 1)
                    if att and s < NP:
                        exps(G, s)
                        if not ffn:
                            k = s
                            act.wait_ge(in_w[k % 2], 16 * (k // 2 + 1))
                            dst = w1_h[:, k, :] if k < NE else w2_h[:, k - NE, :]
                            nc.scalar.copy(dst, w_raw[:, k % 2, :]).then_inc(whi_done, 1)
                    for n in ns[1:]:
                        step(F, n)
                    if att and 0 <= s - TLAG < NP:
                        copy_pt(G, s - TLAG)

            act.wait_ge(in_const, N_CONST - 32)
            act.wait_ge(in_first, N_FIRST)
            nc.scalar.activation(tx[:], gx[:], ACT.Tanh).then_inc(tanh_done, 1)
            nc.scalar.activation(tf[:], gf[:], ACT.Tanh).then_inc(tanh_done, 1)
            act.wait_ge(prep_dve, 12)
            for u in range(U_V):
                prep_use(0, u)
            body(0, True, False, True)
            with act.Fori(1, NG - 1) as G:
                body(G, True, True, True)
            body(NG - 1, True, True, False)
            body(NG, False, True, False)

        @block.gpsimd
        def _(pool):
            def rstd(mv, r, done, G):
                nc.gpsimd.tensor_tensor(r[:, 0, :], mv[:, :, 1], eps4[:], ALU.add).then_inc(done, 1)
                pool.wait_ge(done, at(G, 2, 1))
                nc.gpsimd.tensor_tensor(r[:, 1, :], r[:, 0, :], mhalf4[:], ALU.pow).then_inc(done, 1)

            def norm(G, p):
                pool.wait_ge(rec_done, at(G, NP, p + 1))
                v = P[:, p % 4, :, :]
                nc.gpsimd.tensor_tensor(v, v, rec[:, p % 4, :].unsqueeze(2).broadcast_to((128, HG, LK)),
                                        ALU.mult).then_inc(norm_done, 1)

            def step(F, n):
                if n < NCH:
                    pool.wait_ge(hhi_done, at(F, NCH, n + 1))
                    nc.gpsimd.tensor_tensor(H_l[:, n % 4, :], H[:, n % 4, :], H_h[:, n % 4, :].bitcast(F32),
                                            ALU.subtract).then_inc(hlo_done, 1)
                e = experts_done_at(n)
                if e is not None and e >= 1:
                    pool.wait_ge(wy_done, at(F, NE, e + 1))
                    if e >= 2:
                        pool.wait_ge(acc_done, at(F, NE - 1, e - 1))
                    nc.gpsimd.tensor_tensor(acc[:], acc[:], wy[:], ALU.add).then_inc(acc_done, 1)

            def body(G, att, ffn, nxt):
                F = G - 1
                if att:
                    wait(pool, x1_done, at(G, GB, 0))
                    nc.gpsimd.tensor_tensor(xb[:], group_x(G), bo_sb[:].unsqueeze(1).broadcast_to((128, GB, D)),
                                            ALU.add).then_inc(xb_done, 1)
                for s in range(SLOTS):
                    ns = steps_behind(s) if ffn else []
                    for n in ns[:1]:
                        step(F, n)
                    if att and 0 <= s - 1 < NP:
                        norm(G, s - 1)
                    if att and not ffn and s < NP:
                        k = s
                        pool.wait_ge(whi_done, k + 1)
                        dst, hi = (w1_l, w1_h) if k < NE else (w2_l, w2_h)
                        nc.gpsimd.tensor_tensor(dst[:, k % NE, :], w_raw[:, k % 2, :], hi[:, k % NE, :].bitcast(F32),
                                                ALU.subtract).then_inc(wlo_done, 1)
                    if att and nxt and s == 7:
                        pool.wait_ge(ln1_step, at(G + 1, 2, 2))
                        rstd(mv1, rstd1, rstd1_done, G + 1)
                    for n in ns[1:]:
                        step(F, n)
                    if ffn and s == STEP_SLOTS - 1:
                        for n in range(NCH + LAG - BEHIND, NCH + LAG + 1):
                            step(F, n)
                if att:
                    pool.wait_ge(ln2_step, at(G, 2 * GB, 2 * GB))
                    rstd(mv2, rstd2, rstd2_done, G)

            nc.gpsimd.memset(eps4[:], EPS)
            nc.gpsimd.memset(mhalf4[:], -0.5)
            nc.gpsimd.memset(Vm[:], 0.0).then_inc(const_done, 1)
            pool.wait_ge(const_done, 1)
            pool.wait_ge(ln1_step, 2)
            rstd(mv1, rstd1, rstd1_done, 0)
            pool.wait_ge(prep_dve, 17)
            body(0, True, False, True)
            with pool.Fori(1, NG - 1) as G:
                body(G, True, True, True)
            body(NG - 1, True, True, False)
            body(NG, False, True, False)

        @block.vector
        def _(dve):
            v = nc.vector

            def apart():
                v.memset(spare[0:1, :], 0.0)

            def layer1_stats(G):
                for i in range(GB):
                    ins = v.bn_stats(stat1[:, i, :], batch_x(G, i))
                ins.then_inc(ln1_step, 1)
                dve.wait_ge(ln1_step, at(G, 2, 1))
                apart()
                for i in range(GB):
                    ins = v.bn_aggr(mv1[:, i, :], stat1[:, i, :])
                ins.then_inc(ln1_step, 1)

            def normalise(dst, G, mv, r, done, r_done):
                dve.wait_ge(r_done, at(G, 2, 2))
                for i in range(GB):
                    ins = v.tensor_scalar(dst[:, i, :], batch_x(G, i), mv[:, i, 0:1], r[:, 1, i:i + 1],
                                          ALU.subtract, ALU.mult)
                ins.then_inc(done, 1)

            def low_part(dst, bank, bias, hi):
                return v.scalar_tensor_tensor(dst, bank, bias, hi.bitcast(F32), ALU.add, ALU.subtract)

            def prep_use(G, u):
                bank = A[u % 2]
                if u < U_V:
                    dve.wait_ge(hi_done, at(G, NHI, u + 1))
                else:
                    dve.wait_ge(a_ready, at(G, AUSE, u + 1))
                if u == U_Z:
                    ins = v.tensor_tensor(zT_l[:], bank[:], zT_h[:].bitcast(F32), ALU.subtract)
                elif u == U_CTX:
                    ins = v.tensor_tensor(cT_l[:], bank[:, 0:KEYS], cT_h[:].bitcast(F32), ALU.subtract)
                elif u < U_Q:
                    g = u - U_K
                    for r in (slice(32, 64), slice(96, 128)):
                        ins = low_part(Ks[r, g, :], bank[r, 0:KEYS], bk_sb[r, g:g + 1], Ks[r, g, :])
                elif u < U_V:
                    g = u - U_Q
                    r = slice(64, 128)
                    ins = low_part(Qs[r, g, :], bank[r, :], bq_sb[r, g:g + 1], Qs[r, g, :])
                else:
                    i0 = (u - U_V) * 2
                    for i in range(2):
                        dst = Vm[:, i0 + i, :].rearrange("p (j c) -> p j c", j=HG)
                        for g in range(NHG):
                            ins = v.tensor_copy(dst[:, :, 40 * g:40 * g + DK],
                                                bank[0:LK, i * D:(i + 1) * D]
                                                .rearrange("p (j g d) -> p j g d", j=HG, g=NHG)[:, :, g, :])
                ins.then_inc(a_free, 1)

            def keys_of_batch(G, i):
                dve.wait_ge(a_free, at(G, AUSE, U_Q))
                for j in range(HG):
                    ins = v.tensor_scalar(Kb[:, i % 2, :, j, :], Ks[:, :, i * LK:(i + 1) * LK].bitcast(F32),
                                          hm[:, j:j + 1], None, ALU.mult)
                ins.then_inc(kb_done, 1)

            def masked_max(G, p):
                u = U_S + p
                dve.wait_ge(a_ready, at(G, AUSE, u + 1))
                wait(dve, exp_done, at(G, NP, p - 1))
                v.tensor_tensor(SM[:, p % 2, :, :], A[u % 2][:, 0:HG * LK].rearrange("p (j k) -> p j k", j=HG),
                                mbias[:].unsqueeze(1).broadcast_to((128, HG, LK)), ALU.add).then_inc(a_free, 1)
                dve.wait_ge(a_free, at(G, AUSE, u + 1))
                v.tensor_reduce(nmax[:, p % 4, :], SM[:, p % 2, :, :], AX_X, ALU.max, negate=True).then_inc(max_done, 1)

            def reciprocals(G, p):
                dve.wait_ge(exp_done, at(G, NP, p + 1))
                v.reciprocal(rec[:, p % 4, :], sums[:, p % 4, :]).then_inc(rec_done, 1)

            def residual(G, i):
                dve.wait_ge(proj_done, at(G, GB, i + 1))
                dve.wait_ge(xb_done, at(G, 1, 1))
                v.tensor_tensor(batch_x(G, i), Ob[:, LQ:LQ + D], xb[:, i, :], ALU.add).then_inc(x1_done, 1)
                dve.wait_ge(x1_done, at(G, GB, i + 1))
                apart()
                v.bn_stats(stat2[:, i, :], batch_x(G, i)).then_inc(ln2_step, 1)
                dve.wait_ge(ln2_step, at(G, 2 * GB, 2 * i + 1))
                apart()
                v.bn_aggr(mv2[:, i, :], stat2[:, i, :]).then_inc(ln2_step, 1)

            def route(F, half):
                count = [5 * half]

                def then(ins, needed=True):
                    count[0] += 1
                    ins.then_inc(route_step, 1)
                    if needed:
                        dve.wait_ge(route_step, at(F, ROUTE, count[0]))

                if half == 0:
                    dve.wait_ge(f_ready, at(F, FMUSE, 2))
                    then(v.tensor_tensor(gs[:], Fb[:, 0:GB * NE].rearrange("p (i e) -> p i e", i=GB),
                                         bg_sb[:].unsqueeze(1).broadcast_to((128, GB, NE)), ALU.add))
                    apart()
                    for i in range(GB):
                        ins = v.max(top[:, i, :], gs[:, i, :])
                    then(ins)
                    apart()
                    for i in range(GB):
                        ins = v.max_index(idx[:, i, :], top[:, i, :], gs[:, i, :])
                    then(ins)
                    then(v.tensor_copy(idxf[:], idx[:, :, 0:2]), False)
                    then(v.tensor_tensor(diff[:], top[:, :, 1], top[:, :, 0], ALU.subtract))
                    assert count[0] == 5
                    return
                io = iota_sb[:].unsqueeze(1).broadcast_to((128, GB, NE))
                wide = lambda a: a.unsqueeze(2).broadcast_to((128, GB, NE))
                then(v.tensor_tensor(eq1[:, 0, :, :], io, wide(idxf[:, :, 0]), ALU.is_equal), False)
                then(v.tensor_tensor(eq2[:, 0, :, :], io, wide(idxf[:, :, 1]), ALU.is_equal), False)
                dve.wait_ge(ediff_done, at(F, 1, 1))
                then(v.tensor_scalar(esum[:], ediff[:], 1.0, None, ALU.add))
                then(v.reciprocal(p1[:, 0, :], esum[:]))
                then(v.tensor_scalar(p1[:, 1, :], p1[:, 0, :], tf[:, 0:1], None, ALU.mult))
                then(v.tensor_tensor(p2[:], p1[:, 1, :], ediff[:], ALU.mult), False)
                then(v.tensor_tensor(eq1[:, 1, :, :], eq1[:, 0, :, :], wide(p1[:, 1, :]), ALU.mult))
                then(v.tensor_tensor(eq2[:, 1, :, :], eq2[:, 0, :, :], wide(p2[:]), ALU.mult))
                then(v.tensor_tensor(comb[:], eq1[:, 1, :, :], eq2[:, 1, :, :], ALU.add))
                then(v.tensor_copy(c2[:, :, 0:NE].bitcast(F32R), comb[:]))
                then(v.tensor_tensor(c2[:, :, NE:2 * NE], comb[:], c2[:, :, 0:NE], ALU.subtract), False)
                assert count[0] == ROUTE

            def step(F, n):
                if n < NCH:
                    dve.wait_ge(h_done, at(F, NCH, n + 1))
                    v.tensor_copy(H_h[:, n % 4, :], H[:, n % 4, :]).then_inc(hhi_done, 1)
                e = experts_done_at(n)
                if e is not None:
                    dve.wait_ge(yb_done, at(F, NE, e + 1))
                    dve.wait_ge(f_ready, at(F, FMUSE, 4 + e))
                    if e >= 2:
                        dve.wait_ge(acc_done, at(F, NE - 1, e - 1))
                    v.tensor_tensor((wy if e else acc)[:], yb[:], Fb[:], ALU.mult).then_inc(wy_done, 1)

            def body(G, att, ffn, nxt):
                F = G - 1
                if att:
                    prep_use(G, U_V)
                    prep_use(G, U_V + 1)
                if ffn:
                    dve.wait_ge(z2hi_done, at(F, 1, 1))
                    v.tensor_tensor(z2T_l[:], Fb[:], z2T_h[:].bitcast(F32), ALU.subtract).then_inc(z2lo_done, 1)
                for s in range(SLOTS):
                    ns = steps_behind(s) if ffn else []
                    if att and s < NP:
                        masked_max(G, s)
                    if att and 0 <= s - 1 < NP:
                        reciprocals(G, s - 1)
                    us = NEXT_USES.get(s, []) if nxt else []
                    for u in us[:1]:
                        prep_use(G + 1, u)
                    if att and closes_batch(s) is not None:
                        residual(G, closes_batch(s))
                    for u in us[1:]:
                        prep_use(G + 1, u)
                    if nxt and s == KEYS0_SLOT:
                        keys_of_batch(G + 1, 0)
                    for n in ns[:1]:
                        step(F, n)
                    if att and s < NP and s % NHG == 0 and s // NHG + 1 < GB:
                        keys_of_batch(G, s // NHG + 1)
                    if att and nxt and s == 6:
                        if isinstance(G, int) and G == 0:
                            dve.wait_ge(in_x, N_XREST)
                        layer1_stats(G + 1)
                    if att and nxt and s == 9:
                        normalise(z1, G + 1, mv1, rstd1, z1_done, rstd1_done)
                    for n in ns[1:]:
                        step(F, n)
                    if ffn and s == ROUTE_1:
                        route(F, 0)
                    if ffn and s == ROUTE_2:
                        route(F, 1)
                    if ffn and s == STEP_SLOTS - 1:
                        for n in range(NCH + LAG - BEHIND, NCH + LAG + 1):
                            step(F, n)
                    if ffn and s == RESULT_SLOT:
                        dve.wait_ge(f_ready, at(F, FMUSE, FMUSE))
                        v.tensor_tensor(group_x(F), group_x(F), Fb[:].rearrange("p (i d) -> p i d", i=GB),
                                        ALU.add).then_inc(fin_done, 1)
                if att:
                    normalise(z2, G, mv2, rstd2, z2_done, rstd2_done)

            done = [0]

            def made(ins, needed=True):
                done[0] += 1
                ins.then_inc(prep_dve, 1)
                if needed:
                    dve.wait_ge(prep_dve, done[0])

            dve.wait_ge(in_first, N_FIRST)
            isq = 1.0 / float(DK) ** 0.5
            made(v.tensor_copy(wk_h[:], wk_raw), False)
            layer1_stats(0)
            made(v.tensor_scalar(wq_raw, wq_raw, isq, None, ALU.mult), False)
            made(v.tensor_scalar(bq_sb[:], bq_sb[:], isq, None, ALU.mult))
            made(v.tensor_tensor(wk_l[:], wk_raw, wk_h[:].bitcast(F32), ALU.subtract), False)
            made(v.tensor_copy(wq_h[:], wq_raw), False)
            made(v.tensor_copy(wv_h[:], wv_raw))
            made(v.tensor_tensor(wq_l[:], wq_raw, wq_h[:].bitcast(F32), ALU.subtract), False)
            made(v.tensor_tensor(wv_l[:], wv_raw, wv_h[:].bitcast(F32), ALU.subtract), False)
            normalise(z1, 0, mv1, rstd1, z1_done, rstd1_done)
            dve.wait_ge(in_const, N_CONST - 32)
            made(v.tensor_scalar(mbias[:], mask_i, 0.0, MASKED, ALU.is_equal, ALU.mult))
            made(v.tensor_reduce(mtmp[:, 0:1], mbias[:], AX_X, ALU.max))
            made(v.tensor_scalar(mtmp[:, 1:2], mtmp[:, 0:1], 0.0, None, ALU.is_equal))
            made(v.reciprocal(mtmp[:, 2:3], mtmp[:, 1:2]))
            made(v.tensor_tensor(mtmp[:, 3:4], mtmp[:, 1:2], mtmp[:, 2:3], ALU.mult))
            made(v.tensor_scalar(mbias[:], mbias[:], mtmp[:, 3:4], None, ALU.mult), False)
            made(v.tensor_copy(wg_h[:], wg_raw[:]))
            dve.wait_ge(tanh_done, 2)
            made(v.tensor_scalar(wo_sb[:], wo_sb[:], tx[:, 0:1], None, ALU.mult), False)
            made(v.tensor_scalar(bo_sb[:], bo_sb[:], tx[:, 0:1], None, ALU.mult), False)
            made(v.tensor_tensor(wg_l[:], wg_raw[:], wg_h[:].bitcast(F32), ALU.subtract), False)
            made(v.tensor_copy(sel_r[:], sel_raw))
            for u in range(U_V):
                prep_use(0, u)
            keys_of_batch(0, 0)
            dve.wait_ge(const_done, 1)
            body(0, True, False, True)
            with dve.Fori(1, NG - 1) as G:
                body(G, True, True, True)
            body(NG - 1, True, True, False)
            body(NG, False, True, False)


def kernel(x, ctx_1024, mask_SxS2_ik0, g_xattn, g_ffn, L0_xattn_Wq, L0_xattn_bq, L0_xattn_Wk, L0_xattn_bk,
           L0_xattn_Wv, L0_xattn_bv, L0_xattn_Wo, L0_xattn_bo, L0_ffn_gate_w, L0_ffn_gate_b, L0_ffn_w1,
           L0_ffn_b1, L0_ffn_w2, L0_ffn_b2):
    import numpy as np
    import concourse.bacc as bacc
    from concourse.bass_utils import run_bass_kernel_spmd

    r = np.arange(128)
    rows = np.stack([(4 * (r // 8 % 4) + g) * DK + r % DK for g in range(NHG)])

    def stacked(w):
        return np.ascontiguousarray(np.transpose(np.asarray(w)[rows], (2, 0, 1)))

    def stacked_bias(b):
        return np.ascontiguousarray(np.asarray(b)[rows].T)

    sel = np.zeros((2 * NE, NE, 128), np.float32)
    sel[np.arange(NE), np.arange(NE)] = 1
    sel[NE + np.arange(NE), np.arange(NE)] = 1
    hmask = (r[:, None] // 8 % 4 == np.arange(HG)[None, :]).astype(np.float32)
    c = np.ascontiguousarray
    a = np.asarray
    arrays = {
        "x": c(x), "ctx": c(ctx_1024), "mask": c(mask_SxS2_ik0), "g_x": c(g_xattn), "g_f": c(g_ffn),
        "wq": stacked(L0_xattn_Wq), "bq": stacked_bias(L0_xattn_bq),
        "wk": stacked(L0_xattn_Wk), "bk": stacked_bias(L0_xattn_bk),
        "wv": c(a(L0_xattn_Wv).T), "bv": c(a(L0_xattn_bv).reshape(D, 1)),
        "wo": c(a(L0_xattn_Wo).T), "bo": c(L0_xattn_bo),
        "gate_w": c(L0_ffn_gate_w), "gate_b": c(L0_ffn_gate_b),
        "w1": c(L0_ffn_w1), "b1": c(a(L0_ffn_b1).reshape(NE * NC, 128).T),
        "w2": c(L0_ffn_w2), "b2": c(a(L0_ffn_b2).T),
        "ident": np.eye(128, dtype=np.float32), "sel": sel, "iota": np.arange(NE, dtype=np.float32),
        "hmask": hmask,
    }
    nc = bacc.Bacc("TRN2", target_bir_lowering=False, num_devices=1)
    named, args = {}, []
    for name, v in arrays.items():
        named[f"in_{name}"] = v
        args.append(nc.dram_tensor(f"in_{name}", v.shape, mybir.dt.from_np(v.dtype), kind="ExternalInput").ap())
    out = nc.dram_tensor("out_0", (B, LQ, D), F32, kind="ExternalOutput").ap()
    build(nc, *args, out)
    res = run_bass_kernel_spmd(nc, [named], core_ids=[0])
    return res.results[0]["out_0"]
```
